# Optimizing a Trainium2 kernel written in Bass

```python
import numpy as np
import jax
import jax.numpy as jnp

def _softmax(x, axis=-1):
    return jax.nn.softmax(x, axis=axis)

def _gelu(x):
    return jax.nn.gelu(x, approximate=True)

def _silu(x):
    return jax.nn.silu(x)

def _sigmoid(x):
    return jax.nn.sigmoid(x)

def _layernorm(x, axis=-1, eps=1e-05):
    m = jnp.mean(x, axis=axis, keepdims=True)
    v = jnp.var(x, axis=axis, keepdims=True)
    return (x - m) / jnp.sqrt(v + eps)

def _scatter_add(tgt, idx, src, axis=0):
    return tgt.at[idx].add(src)

def _segment_sum(src, seg, n):
    return jax.ops.segment_sum(src, seg, n)
kernel_name = 'mk_adj_resnorm_d2_adj_r2_0d8848'

def setup_inputs(seed: int=0):
    np.random.seed(seed)
    _w = jnp.asarray

    def _rec_inputs():
        import jax
        import jax.numpy as jnp
        _gk = jax.random.key(seed)
        x = -0.0005207 + 1.001 * jax.random.normal(jax.random.fold_in(_gk, 1), (4096, 128), jnp.float32)
        _a = jax.random.bernoulli(jax.random.fold_in(_gk, 2), 0.00195312, (4096, 4096))
        _a = jnp.logical_or(_a, jnp.swapaxes(_a, -1, -2))
        _a = jnp.logical_or(_a, jnp.eye(4096, dtype=bool))
        _af = _a.astype(jnp.float32)
        _af = _af * jax.random.uniform(jax.random.fold_in(_gk, 3), (4096, 4096), jnp.float32, 0.05, 5.41998)
        adj = _af
        return (x, adj)
    x, adj = _rec_inputs()

    def _L0_gnn_setup():
        import jax, jax.numpy as jnp
        import numpy as np
        N = 4096
        C = 128
        key = jax.random.key(seed)
        k1, k2, k3 = jax.random.split(key, 3)
        x = jax.random.normal(k1, (N, C), dtype=jnp.float32)
        evals = jax.random.uniform(k2, (N,), dtype=jnp.float32)
        evecs = jax.random.normal(k3, (N, N), dtype=jnp.float32)
        t = jnp.ones((1,), dtype=jnp.float32)
        return {'x': x, 'evals': evals, 'evecs': evecs, 't': t}
    _L0_gnn_all = _L0_gnn_setup()
    _L0_gnn_in = {k: v for k, v in _L0_gnn_all.items() if k in ('evals', 't')}
    del _L0_gnn_all

    def _L1_gnn_setup():
        import jax, jax.numpy as jnp
        import numpy as np
        N = 4096
        F_IN = 128
        F_OUT = 128
        key = jax.random.key(seed)
        k1, k2, k3, k4 = jax.random.split(key, 4)
        x = jax.random.normal(k1, (N, F_IN), dtype=jnp.float32)
        adj = jax.random.uniform(k2, (N, N), dtype=jnp.float32)
        bound = 1.0 / np.sqrt(F_IN)
        W = jax.random.uniform(k3, (F_OUT, F_IN), minval=-bound, maxval=bound, dtype=jnp.float32)
        b = jax.random.uniform(k4, (F_OUT,), minval=-bound, maxval=bound, dtype=jnp.float32)
        return {'x': x, 'adj': adj, 'W': W, 'b': b}
    _L1_gnn_all = _L1_gnn_setup()
    _L1_gnn_in = {k: v for k, v in _L1_gnn_all.items() if k in ('W', 'b')}
    del _L1_gnn_all
    return {'x': x, 'adj': adj, 'L0_gnn_evals': _L0_gnn_in['evals'], 'L0_gnn_t': _L0_gnn_in['t'], 'L1_gnn_W': _L1_gnn_in['W'], 'L1_gnn_b': _L1_gnn_in['b']}

def reference(x, adj, L0_gnn_evals, L0_gnn_t, L1_gnn_W, L1_gnn_b):
    import jax
    import jax.numpy as jnp

    def _L0_gnn_ref(x, evals, evecs, t):
        import jax, jax.numpy as jnp
        import numpy as np
        N = 4096
        C = 128
        t_eff = jnp.clip(t[0], 1e-08, None)
        x_spec = jnp.einsum('nk,nc->kc', evecs, x)
        coefs = jnp.exp(-evals * t_eff)[:, None]
        out = jnp.einsum('nk,kc->nc', evecs, coefs * x_spec)
        return out

    def _L1_gnn_ref(x, adj, W, b):
        import jax, jax.numpy as jnp
        import numpy as np
        N = 4096
        F_IN = 128
        F_OUT = 128
        rowsum = adj.sum(axis=1)
        d_inv_sqrt = jnp.power(rowsum, -0.5)
        d_inv_sqrt = jnp.where(jnp.isinf(d_inv_sqrt), 0.0, d_inv_sqrt)
        adj_norm = d_inv_sqrt[:, None] * adj * d_inv_sqrt[None, :]
        h = adj_norm @ x
        return h @ W.T + b
    x = _layernorm(x + _L0_gnn_ref(x, L0_gnn_evals, adj, L0_gnn_t), axis=-1)
    x = _layernorm(x + _L1_gnn_ref(x, adj, L1_gnn_W, L1_gnn_b), axis=-1)
    return x

_drawn_inputs = setup_inputs


def setup_inputs(seed=0):
    import zlib

    import numpy as np

    out = dict(_drawn_inputs(seed))
    spreads = {}
    factors = {}
    for name, (base, spread) in spreads.items():
        noise = np.random.default_rng([zlib.crc32(name.encode()), seed]).standard_normal(out[name].shape)
        drawn = base * np.exp(spread * noise) if base else spread * noise
        out[name] = jnp.asarray(drawn.astype(out[name].dtype))
    for name, factor in factors.items():
        out[name] = (out[name] * factor).astype(out[name].dtype)
    return out
```

```python
import concourse.bass as bass
from concourse import mybir
from contextlib import ExitStack


def spectral_gcn_kernel(
    nc: bass.Bass,
    x: bass.AP,
    adj: bass.AP,
    adj_t: bass.AP,
    evals: bass.AP,
    t: bass.AP,
    w_t: bass.AP,
    b: bass.AP,
    out: bass.AP,
):
    fp32 = mybir.dt.float32
    fp32r = mybir.dt.float32r
    ALU = mybir.AluOpType
    ACT = mybir.ActivationFunctionType

    P = nc.NUM_PARTITIONS
    N, C = x.shape
    TILES = N // P
    BANKS = 8
    BANK = N // BANKS
    GROUP = BANK // P
    GROUPS = TILES // GROUP
    RAW = GROUP
    HALVES = 2
    HALF = N // HALVES
    HALF_BANKS = BANKS // HALVES
    SPLIT = 4
    STAT = GROUP
    EVAC = 2
    EPS = 1e-5
    LAST = TILES * HALVES

    x_v = x.rearrange("(t p) c -> p t c", p=P)
    out_v = out.rearrange("(t p) c -> p t c", p=P)

    ctx = ExitStack()
    with ctx:
        def sb(name, shape, dt=fp32):
            return ctx.enter_context(nc.sbuf_tensor(name, shape, dt))

        def sem(name):
            return ctx.enter_context(nc.semaphore(name))

        raw = [sb(f"raw{s}", [P, N]) for s in range(RAW)]
        high = [sb(f"high{s}", [P, HALF], fp32r) for s in range(SPLIT)]
        low = [sb(f"low{s}", [P, HALF], fp32r) for s in range(SPLIT)]
        stat_high = [sb(f"stat_high{s}", [P, C], fp32r) for s in range(STAT)]
        stat_low = [sb(f"stat_low{s}", [P, C], fp32r) for s in range(STAT)]
        nodes = sb("nodes", [P, TILES, C])
        scaled = sb("scaled", [P, TILES, C])
        evac = [sb(f"evac{s}", [P, BANK]) for s in range(EVAC)]
        result = [sb(f"result{s}", [P, GROUP, C]) for s in range(2)]
        identity = sb("identity", [P, P])
        w_t_sb = sb("w_t_sb", [C, C])
        bias_row = sb("bias_row", [P, C])
        evals_sb = sb("evals_sb", [P, TILES])
        t_sb = sb("t_sb", [P, 1])
        t_eff = sb("t_eff", [P, 1])
        decay = sb("decay", [P, TILES])
        coefs = sb("coefs", [P, TILES])
        row_parts = sb("row_parts", [P, TILES, HALVES])
        row_sum = sb("row_sum", [P, TILES])
        row_zero = sb("row_zero", [P, TILES])
        row_safe = sb("row_safe", [P, TILES])
        row_keep = sb("row_keep", [P, TILES])
        row_pow = sb("row_pow", [P, TILES])
        d_inv = sb("d_inv", [P, TILES])
        minus_half = sb("minus_half", [P, TILES])
        stats = sb("stats", [P, 2, GROUP, 6])
        moments = sb("moments", [P, 2, GROUP, 2])
        var_eps = sb("var_eps", [P, 2, GROUP])
        rstd = sb("rstd", [P, 2, GROUP])

        psum = [ctx.enter_context(nc.psum_tensor(f"bank{k}", [P, BANK], fp32)) for k in range(BANKS)]

        x_loaded = sem("x_loaded")
        small_loaded = sem("small_loaded")
        weights_loaded = sem("weights_loaded")
        raw_loaded = [sem(f"raw_loaded{s}") for s in range(RAW)]
        high_ready = sem("high_ready")
        low_ready = sem("low_ready")
        stat_ready = sem("stat_ready")
        products_done = sem("products_done")
        constants_ready = sem("constants_ready")
        decay_step = sem("decay_step")
        coefs_ready = sem("coefs_ready")
        evacuated = sem("evacuated")
        turned = sem("turned")
        scaled_ready = sem("scaled_ready")
        bank_read = sem("bank_read")
        row_step = sem("row_step")
        row_pow_ready = sem("row_pow_ready")
        d_inv_ready = sem("d_inv_ready")
        norm_step = sem("norm_step")
        var_ready = sem("var_ready")
        rstd_ready = sem("rstd_ready")
        normed = sem("normed")
        bias_added = sem("bias_added")
        result_ready = sem("result_ready")
        stored = [sem(f"stored{s}") for s in range(2)]

        block = ctx.enter_context(nc.Block())

        def first_tile(pas):
            return RAW if pas == 1 else 0

        def raw_round(pas, g):
            return (g + 1, g + 1 + GROUPS, g + 2 * GROUPS)[pas]

        def turn_order(pas):
            return [(k + first_tile(pas + 1) // GROUP) % BANKS for k in range(BANKS)]

        @block.sync
        def _(sp):
            def load(source, pas, g, m, row):
                if not (pas == 0 and isinstance(g, int) and g == 0):
                    sp.wait_ge(low_ready, (g * GROUP + (pas * TILES + m - RAW + 1)) * HALVES)
                sp.dma_start(raw[m][:, :], source[bass.ds(row, P), :]).then_inc(raw_loaded[m], 16)

            for m in range(GROUP):
                load(adj, 0, 0, m, m * P)
            with sp.Fori(1, GROUPS) as g:
                for m in range(GROUP):
                    load(adj, 0, g, m, (g * GROUP + m) * P)
            with sp.Fori(0, GROUPS - 1) as g:
                for m in range(GROUP):
                    load(adj_t, 1, g, m, (g * GROUP + m + RAW) * P)
            for m in range(GROUP):
                load(adj_t, 1, GROUPS - 1, m, m * P)
            with sp.Fori(1, GROUPS) as g:
                for m in range(GROUP):
                    load(adj_t, 2, g, m, (g * GROUP + m) * P)

            for k in range(BANKS):
                sp.wait_ge(result_ready, k + 1)
                sp.dma_start(out_v[:, k * GROUP:(k + 1) * GROUP, :], result[k % 2][:, :, :])\
                    .then_inc(stored[k % 2], 16)
            for s in range(2):
                sp.wait_ge(stored[s], 16 * BANKS // 2)

        @block.scalar
        def _(act):
            act.dma_start(nodes[:, :, :], x_v).then_inc(x_loaded, 16)
            act.dma_start(evals_sb[:, :], evals).then_inc(small_loaded, 16)
            act.dma_start(t_sb[:, :], t.partition_broadcast(P)).then_inc(small_loaded, 16)
            act.dma_start(w_t_sb[:, :], w_t).then_inc(weights_loaded, 16)
            act.dma_start(bias_row[:, :], b.partition_broadcast(P)).then_inc(weights_loaded, 16)
            act.wait_ge(decay_step, 2)
            act.activation(coefs[:, :], decay[:, :], ACT.Exp).then_inc(coefs_ready, 1)

            def split_high(pas, g, m):
                act.wait_ge(raw_loaded[m], 16 * raw_round(pas, g))
                for h in range(HALVES):
                    u = (g * GROUP + (pas * TILES + m)) * HALVES + h
                    slot = (m * HALVES + h) % SPLIT
                    if not (pas == 0 and isinstance(g, int) and g == 0 and m * HALVES + h < SPLIT):
                        act.wait_ge(products_done, u - (SPLIT - 1))
                    piece = raw[m][:, h * HALF:(h + 1) * HALF]
                    if pas == 0:
                        act.activation(high[slot][:, :], piece, ACT.Copy,
                                       accum_out=row_parts[:, bass.ds(g * GROUP + m, 1), h])\
                            .then_inc(high_ready, 1)
                    else:
                        act.activation(high[slot][:, :], piece, ACT.Copy).then_inc(high_ready, 1)

            def evacuate(pas):
                for n, k in enumerate(turn_order(pas)):
                    c = pas * BANKS + n
                    if n == 0:
                        act.wait_ge(products_done, (pas + 1) * LAST)
                    if c >= EVAC:
                        act.wait_ge(turned, c - EVAC + 1)
                    act.activation(evac[c % EVAC][:, :], psum[k][:, :], ACT.Copy).then_inc(evacuated, 1)

            for m in range(GROUP):
                split_high(0, 0, m)
            with act.Fori(1, GROUPS) as g:
                for m in range(GROUP):
                    split_high(0, g, m)
            for pas in (1, 2):
                evacuate(pas - 1)
                with act.Fori(0, GROUPS) as g:
                    for m in range(GROUP):
                        split_high(pas, g, m)
            evacuate(2)

        @block.tensor
        def _(pe):
            def products(pas, g, m, start=False, stop=False):
                pe.wait_ge(stat_ready, g * GROUP + (pas * TILES + m + 1))
                for h in range(HALVES):
                    u = (g * GROUP + (pas * TILES + m)) * HALVES + h
                    slot = (m * HALVES + h) % SPLIT
                    banks = range(h * HALF_BANKS, (h + 1) * HALF_BANKS)
                    pe.wait_ge(high_ready, u + 1)
                    for k in banks:
                        cols = slice((k % HALF_BANKS) * BANK, (k % HALF_BANKS + 1) * BANK)
                        pe.matmul(psum[k][:, :], stat_low[m][:, :], high[slot][:, cols],
                                  start=start, stop=False)
                    for k in banks:
                        cols = slice((k % HALF_BANKS) * BANK, (k % HALF_BANKS + 1) * BANK)
                        pe.matmul(psum[k][:, :], stat_high[m][:, :], high[slot][:, cols],
                                  start=False, stop=False)
                    pe.wait_ge(low_ready, u + 1)
                    for k in banks:
                        cols = slice((k % HALF_BANKS) * BANK, (k % HALF_BANKS + 1) * BANK)
                        mm = pe.matmul(psum[k][:, :], stat_high[m][:, :], low[slot][:, cols],
                                       start=False, stop=stop)
                    mm.then_inc(products_done, 1)

            def turn(pas):
                for n, k in enumerate(turn_order(pas)):
                    c = pas * BANKS + n
                    pe.wait_ge(evacuated, c + 1)
                    for m in range(GROUP):
                        cols = slice(m * P, (m + 1) * P)
                        mm = pe.transpose(psum[k][:, cols], evac[c % EVAC][:, cols], identity[:, :])
                    mm.then_inc(turned, 1)

            pe.wait_ge(constants_ready, 3)
            for pas in range(3):
                if pas:
                    pe.wait_ge(bank_read, pas * BANKS)
                for m in range(GROUP):
                    products(pas, 0, m, start=(m == 0))
                with pe.Fori(1, GROUPS - 1) as g:
                    for m in range(GROUP):
                        products(pas, g, m)
                for m in range(GROUP):
                    products(pas, GROUPS - 1, m, stop=(m == GROUP - 1))
                if pas < 2:
                    turn(pas)
            pe.wait_ge(weights_loaded, 32)
            for k in range(BANKS):
                c = 2 * BANKS + k
                pe.wait_ge(evacuated, c + 1)
                for m in range(GROUP):
                    cols = slice(m * P, (m + 1) * P)
                    mm = pe.matmul(psum[k][:, cols], evac[c % EVAC][:, cols], w_t_sb[:, :],
                                   start=True, stop=True)
                mm.then_inc(turned, 1)

        @block.gpsimd
        def _(pool):
            pool.memset(minus_half[:, :], -0.5).then_inc(constants_ready, 1)
            pool.memset(identity[:, :], 0.0).then_inc(constants_ready, 1)
            pool.wait_ge(constants_ready, 2)
            pool.affine_select(out=identity[:, :], in_=identity[:, :], compare_op=ALU.not_equal, fill=1.0,
                               base=0, pattern=[[-1, P]], channel_multiplier=1)\
                .then_inc(constants_ready, 1)

            def split_stationary(pas, g, m):
                source = nodes if pas == 0 else scaled
                tile = g * GROUP + (m + first_tile(pas))
                q = g * GROUP + (pas * TILES + m)
                if isinstance(tile, int):
                    tile %= TILES
                pool.wait_ge(x_loaded, 16)
                if not (pas == 0 and isinstance(g, int) and g == 0):
                    pool.wait_ge(products_done, (q - (STAT - 1)) * HALVES)
                pool.tensor_copy(stat_high[m][:, :], source[:, bass.ds(tile, 1), :].rearrange("p a c -> p (a c)"))
                pool.drain()
                pool.tensor_tensor(stat_low[m][:, :], source[:, bass.ds(tile, 1), :].rearrange("p a c -> p (a c)"),
                                   stat_high[m][:, :].bitcast(fp32), ALU.subtract).then_inc(stat_ready, 1)

            def rstds(c):
                pool.wait_ge(var_ready, c + 1)
                pool.tensor_tensor(rstd[:, c % 2, :], var_eps[:, c % 2, :], minus_half[:, 0:GROUP], ALU.pow)\
                    .then_inc(rstd_ready, 1)

            pool.wait_ge(x_loaded, 16)
            for m in range(GROUP):
                split_stationary(0, 0, m)
            with pool.Fori(1, GROUPS) as g:
                for m in range(GROUP):
                    split_stationary(0, g, m)
            pool.wait_ge(row_step, 4)
            pool.tensor_tensor(row_pow[:, :], row_safe[:, :], minus_half[:, :], ALU.pow).then_inc(row_pow_ready, 1)
            with pool.Fori(0, GROUPS - 1) as g:
                pool.wait_ge(scaled_ready, g + 1)
                for m in range(GROUP):
                    split_stationary(1, g, m)
            pool.wait_ge(scaled_ready, BANKS)
            for m in range(GROUP):
                split_stationary(1, GROUPS - 1, m)
            for k in range(BANKS):
                rstds(k)
                pool.wait_ge(normed, k + 1)
                if k == 0:
                    pool.wait_ge(d_inv_ready, 1)
                tiles = slice(k * GROUP, (k + 1) * GROUP)
                pool.tensor_tensor(scaled[:, tiles, :], nodes[:, tiles, :],
                                   d_inv[:, tiles].unsqueeze(2).broadcast_to([P, GROUP, C]), ALU.mult)\
                    .then_inc(scaled_ready, 1)
            pool.wait_ge(scaled_ready, 2 * BANKS)
            with pool.Fori(0, GROUPS) as g:
                for m in range(GROUP):
                    split_stationary(2, g, m)
            pool.wait_ge(weights_loaded, 32)
            for tile in range(TILES):
                add = pool.tensor_tensor(nodes[:, tile, :], nodes[:, tile, :], bias_row[:, :], ALU.add)
            add.then_inc(bias_added, 1)
            for k in range(BANKS):
                rstds(BANKS + k)

        @block.vector
        def _(dve):
            dve.wait_ge(small_loaded, 32)
            dve.tensor_scalar(t_eff[:, :], t_sb[:, :], 1e-8, -1.0, ALU.max, ALU.mult).then_inc(decay_step, 1)
            dve.wait_ge(decay_step, 1)
            dve.tensor_scalar(decay[:, :], evals_sb[:, :], t_eff[:, 0:1], None, ALU.mult).then_inc(decay_step, 1)

            def split_low(pas, g, m):
                for h in range(HALVES):
                    u = (g * GROUP + (pas * TILES + m)) * HALVES + h
                    slot = (m * HALVES + h) % SPLIT
                    dve.wait_ge(high_ready, u + 1)
                    dve.tensor_tensor(low[slot][:, :], raw[m][:, h * HALF:(h + 1) * HALF],
                                      high[slot][:, :].bitcast(fp32), ALU.subtract).then_inc(low_ready, 1)

            steps = [0]

            def step_done(instruction):
                instruction.then_inc(norm_step, 1)
                steps[0] += 1
                dve.wait_ge(norm_step, steps[0])

            def normalise(c, rows, to):
                s = c % 2
                for m in range(GROUP):
                    last = dve.bn_stats(stats[:, s, m, :], rows[:, m, :])
                step_done(last)
                for m in range(GROUP):
                    last = dve.bn_aggr(moments[:, s, m, :], stats[:, s, m, :])
                step_done(last)
                dve.tensor_scalar(var_eps[:, s, :], moments[:, s, :, 1], EPS, None, ALU.add)\
                    .then_inc(var_ready, 1)
                dve.wait_ge(rstd_ready, c + 1)
                for m in range(GROUP):
                    last = dve.tensor_scalar(to[:, m, :], rows[:, m, :], moments[:, s, m, 0:1],
                                             rstd[:, s, m:m + 1], ALU.subtract, ALU.mult)
                return last

            def bank(k):
                return psum[k][:, :].rearrange("p (m c) -> p m c", m=GROUP)

            def spread(column, tiles):
                return column[:, tiles].unsqueeze(2).broadcast_to([P, GROUP, C])

            with dve.Fori(0, GROUPS) as g:
                for m in range(GROUP):
                    split_low(0, g, m)

            dve.wait_ge(coefs_ready, 1)
            for n, k in enumerate(turn_order(0)):
                tiles = slice(k * GROUP, (k + 1) * GROUP)
                dve.wait_ge(turned, n + 1)
                last = dve.tensor_tensor(scaled[:, tiles, :], bank(k), spread(coefs, tiles), ALU.mult)
                last.then_inc(scaled_ready, 1)
                dve.wait_ge(scaled_ready, n + 1)
                dve.sem_inc(bank_read, 1)

            dve.tensor_tensor(row_sum[:, :], row_parts[:, :, 0], row_parts[:, :, 1], ALU.add).then_inc(row_step, 1)
            dve.wait_ge(row_step, 1)
            dve.tensor_scalar(row_zero[:, :], row_sum[:, :], 0.0, None, ALU.is_equal).then_inc(row_step, 1)
            dve.tensor_scalar(row_keep[:, :], row_sum[:, :], 0.0, None, ALU.not_equal).then_inc(row_step, 1)
            dve.wait_ge(row_step, 3)
            dve.tensor_tensor(row_safe[:, :], row_sum[:, :], row_zero[:, :], ALU.add).then_inc(row_step, 1)

            with dve.Fori(0, GROUPS) as g:
                for m in range(GROUP):
                    split_low(1, g, m)

            dve.wait_ge(row_pow_ready, 1)
            dve.tensor_tensor(d_inv[:, :], row_pow[:, :], row_keep[:, :], ALU.mult).then_inc(d_inv_ready, 1)
            for k in turn_order(1):
                rows = nodes[:, k * GROUP:(k + 1) * GROUP, :]
                dve.wait_ge(turned, BANKS + k + 1)
                step_done(dve.tensor_tensor(rows, bank(k), rows, ALU.add))
                dve.sem_inc(bank_read, 1)
                normalise(k, rows, rows).then_inc(normed, 1)

            with dve.Fori(0, GROUPS) as g:
                for m in range(GROUP):
                    split_low(2, g, m)

            dve.wait_ge(bias_added, 1)
            for k in range(BANKS):
                tiles = slice(k * GROUP, (k + 1) * GROUP)
                rows = scaled[:, tiles, :]
                dve.wait_ge(turned, 2 * BANKS + k + 1)
                step_done(dve.tensor_tensor(rows, bank(k), spread(d_inv, tiles), ALU.mult))
                step_done(dve.tensor_tensor(rows, rows, nodes[:, tiles, :], ALU.add))
                if k >= 2:
                    dve.wait_ge(stored[k % 2], 16 * (k // 2))
                normalise(BANKS + k, rows, result[k % 2][:, :, :]).then_inc(result_ready, 1)


def kernel(**inputs):
    import numpy as _np
    import concourse.bacc as _bacc
    from concourse import mybir as _mybir
    from concourse.bass_utils import run_bass_kernel_spmd as _run

    x, adj = _np.asarray(inputs["x"]), _np.asarray(inputs["adj"])
    n, c = x.shape
    partitions = 128
    laid_out = {
        "x": x,
        "adj": adj,
        "adj_t": adj.T,
        "evals": _np.asarray(inputs["L0_gnn_evals"]).reshape(n // partitions, partitions).T,
        "t": _np.asarray(inputs["L0_gnn_t"]),
        "w_t": _np.asarray(inputs["L1_gnn_W"]).T,
        "b": _np.asarray(inputs["L1_gnn_b"]),
    }
    nc = _bacc.Bacc("TRN2", target_bir_lowering=False, num_devices=1)
    arrays, args = {}, []
    for name, a in laid_out.items():
        a = _np.ascontiguousarray(a)
        arrays[f"in_{name}_dram"] = a
        args.append(nc.dram_tensor(f"in_{name}_dram", a.shape, _mybir.dt.from_np(a.dtype), kind="ExternalInput").ap())
    args.append(nc.dram_tensor("out_0_dram", (n, c), _mybir.dt.float32, kind="ExternalOutput").ap())
    spectral_gcn_kernel(nc, *args)
    r = _run(nc, [arrays], core_ids=[0])
    return r.results[0]["out_0_dram"]
```

```python
import concourse.bass as bass
from concourse import mybir
from contextlib import ExitStack


def spectral_gcn_kernel(
    nc: bass.Bass,
    x: bass.AP,
    adj: bass.AP,
    adj_t: bass.AP,
    evals: bass.AP,
    t: bass.AP,
    w_t: bass.AP,
    b: bass.AP,
    out: bass.AP,
):
    fp32 = mybir.dt.float32
    fp32r = mybir.dt.float32r
    ALU = mybir.AluOpType
    ACT = mybir.ActivationFunctionType

    P = nc.NUM_PARTITIONS
    N, C = x.shape
    TILES = N // P
    BANKS = 8
    BANK = N // BANKS
    GROUP = BANK // P
    GROUPS = TILES // GROUP
    RAW = GROUP
    HALVES = 2
    HALF = N // HALVES
    HALF_BANKS = BANKS // HALVES
    SPLIT = 4
    STAT = GROUP
    EVAC = 3
    TURN_LAG = 2
    PEELED = BANKS // GROUP + 1
    EPS = 1e-5
    LAST = TILES * HALVES

    x_v = x.rearrange("(t p) c -> p t c", p=P)
    out_v = out.rearrange("(t p) c -> p t c", p=P)

    ctx = ExitStack()
    with ctx:
        def sb(name, shape, dt=fp32):
            return ctx.enter_context(nc.sbuf_tensor(name, shape, dt))

        def sem(name):
            return ctx.enter_context(nc.semaphore(name))

        raw = [sb(f"raw{s}", [P, N]) for s in range(RAW)]
        high = [sb(f"high{s}", [P, HALF], fp32r) for s in range(SPLIT)]
        low = [sb(f"low{s}", [P, HALF], fp32r) for s in range(SPLIT)]
        stat_high = [sb(f"stat_high{s}", [P, C], fp32r) for s in range(STAT)]
        stat_low = [sb(f"stat_low{s}", [P, C], fp32r) for s in range(STAT)]
        nodes = sb("nodes", [P, TILES, C])
        scaled = sb("scaled", [P, TILES, C])
        evac = [sb(f"evac{s}", [P, BANK]) for s in range(EVAC)]
        result = [sb(f"result{s}", [P, GROUP, C]) for s in range(2)]
        identity = sb("identity", [P, P])
        w_t_sb = sb("w_t_sb", [C, C])
        bias_row = sb("bias_row", [P, C])
        evals_sb = sb("evals_sb", [P, TILES])
        t_sb = sb("t_sb", [P, 1])
        t_eff = sb("t_eff", [P, 1])
        decay = sb("decay", [P, TILES])
        coefs = sb("coefs", [P, TILES])
        row_parts = sb("row_parts", [P, TILES, HALVES])
        row_sum = sb("row_sum", [P, TILES])
        row_zero = sb("row_zero", [P, TILES])
        row_safe = sb("row_safe", [P, TILES])
        row_keep = sb("row_keep", [P, TILES])
        row_pow = sb("row_pow", [P, TILES])
        d_inv = sb("d_inv", [P, TILES])
        minus_half = sb("minus_half", [P, TILES])
        stats = sb("stats", [P, 2, GROUP, 6])
        moments = sb("moments", [P, 2, GROUP, 2])
        var_eps = sb("var_eps", [P, 2, GROUP])
        rstd = sb("rstd", [P, 2, GROUP])

        psum = [ctx.enter_context(nc.psum_tensor(f"bank{k}", [P, BANK], fp32)) for k in range(BANKS)]

        x_loaded = sem("x_loaded")
        x_rest_loaded = sem("x_rest_loaded")
        half_loaded = sem("half_loaded")
        small_loaded = sem("small_loaded")
        weights_loaded = sem("weights_loaded")
        raw_loaded = [sem(f"raw_loaded{s}") for s in range(RAW)]
        high_ready = sem("high_ready")
        low_ready = sem("low_ready")
        stat_ready = sem("stat_ready")
        products_done = sem("products_done")
        constants_ready = sem("constants_ready")
        decay_step = sem("decay_step")
        coefs_ready = sem("coefs_ready")
        bank_done = sem("bank_done")
        evacuated = sem("evacuated")
        turned = sem("turned")
        bank_read = sem("bank_read")
        scaled_ready = sem("scaled_ready")
        row_step = sem("row_step")
        row_pow_ready = sem("row_pow_ready")
        d_inv_ready = sem("d_inv_ready")
        norm_step = sem("norm_step")
        var_ready = sem("var_ready")
        rstd_ready = sem("rstd_ready")
        normed = sem("normed")
        bias_added = sem("bias_added")
        result_ready = sem("result_ready")
        stored = [sem(f"stored{s}") for s in range(2)]

        block = ctx.enter_context(nc.Block())

        def first_tile(pas):
            return RAW if pas == 1 else 0

        def raw_round(pas, g):
            return (g + 1, g + 1 + GROUPS, g + 2 * GROUPS)[pas]

        def turn_order(pas):
            first = first_tile(pas + 1) // GROUP
            return [first] + [k for k in range(BANKS) if k != first]

        def groups(engine, start, end, body):
            with engine.Fori(start, end) as g:
                for m in range(GROUP):
                    body(g, m)

        @block.sync
        def _(sp):
            def load(source, pas, g, m, row):
                if not (pas == 0 and isinstance(g, int) and g == 0):
                    sp.wait_ge(low_ready, (g * GROUP + (pas * TILES + m - RAW + 1)) * HALVES)
                sp.dma_start(raw[m][:, :], source[bass.ds(row, P), :]).then_inc(raw_loaded[m], 16)

            sp.dma_start(nodes[:, 0:GROUP, :], x_v[:, 0:GROUP, :]).then_inc(x_loaded, 16)
            sp.dma_start(raw[0][:, 0:HALF], adj[0:P, 0:HALF]).then_inc(half_loaded, 16)
            sp.dma_start(raw[0][:, HALF:N], adj[0:P, HALF:N]).then_inc(raw_loaded[0], 16)
            load(adj, 0, 0, 1, P)
            sp.dma_start(nodes[:, GROUP:TILES, :], x_v[:, GROUP:TILES, :]).then_inc(x_rest_loaded, 16)
            for m in range(2, GROUP):
                load(adj, 0, 0, m, m * P)
            with sp.Fori(1, GROUPS) as g:
                for m in range(GROUP):
                    load(adj, 0, g, m, (g * GROUP + m) * P)
            with sp.Fori(0, GROUPS - 1) as g:
                for m in range(GROUP):
                    load(adj_t, 1, g, m, (g * GROUP + m + RAW) * P)
            for m in range(GROUP):
                load(adj_t, 1, GROUPS - 1, m, m * P)
            with sp.Fori(1, GROUPS) as g:
                for m in range(GROUP):
                    load(adj_t, 2, g, m, (g * GROUP + m) * P)

            for k in range(BANKS):
                sp.wait_ge(result_ready, k + 1)
                sp.dma_start(out_v[:, k * GROUP:(k + 1) * GROUP, :], result[k % 2][:, :, :])\
                    .then_inc(stored[k % 2], 16)
            for s in range(2):
                sp.wait_ge(stored[s], 16 * BANKS // 2)

        @block.scalar
        def _(act):
            act.dma_start(evals_sb[:, :], evals).then_inc(small_loaded, 16)
            act.dma_start(t_sb[:, :], t.partition_broadcast(P)).then_inc(small_loaded, 16)
            act.dma_start(w_t_sb[:, :], w_t).then_inc(weights_loaded, 16)
            act.dma_start(bias_row[:, :], b.partition_broadcast(P)).then_inc(weights_loaded, 16)
            act.wait_ge(decay_step, 2)
            act.activation(coefs[:, :], decay[:, :], ACT.Exp).then_inc(coefs_ready, 1)

            def split_high(pas, g, m):
                very_first = pas == 0 and isinstance(g, int) and g == 0
                for h in range(HALVES):
                    if very_first and m == 0 and h == 0:
                        act.wait_ge(half_loaded, 16)
                    else:
                        act.wait_ge(raw_loaded[m], 16 * raw_round(pas, g))
                    u = (g * GROUP + (pas * TILES + m)) * HALVES + h
                    slot = (m * HALVES + h) % SPLIT
                    if not (very_first and m * HALVES + h < SPLIT):
                        act.wait_ge(products_done, u - (SPLIT - 1))
                    piece = raw[m][:, h * HALF:(h + 1) * HALF]
                    if pas == 0:
                        act.activation(high[slot][:, :], piece, ACT.Copy,
                                       accum_out=row_parts[:, bass.ds(g * GROUP + m, 1), h])\
                            .then_inc(high_ready, 1)
                    else:
                        act.activation(high[slot][:, :], piece, ACT.Copy).then_inc(high_ready, 1)

            def evacuate(pas):
                for n, k in enumerate(turn_order(pas)):
                    c = pas * BANKS + n
                    h, behind = divmod(n, HALF_BANKS)
                    if behind == HALF_BANKS - 1:
                        act.wait_ge(products_done, (pas + 1) * LAST - HALVES + h + 1)
                    else:
                        act.wait_ge(bank_done, (pas * HALVES + h) * (HALF_BANKS - 1) + behind + 1)
                    if c >= EVAC:
                        act.wait_ge(turned, c - EVAC + 1)
                    act.activation(evac[c % EVAC][:, :], psum[k][:, :], ACT.Copy).then_inc(evacuated, 1)

            for m in range(GROUP):
                split_high(0, 0, m)
            groups(act, 1, GROUPS, lambda g, m: split_high(0, g, m))
            for pas in (1, 2):
                split_high(pas, 0, 0)
                evacuate(pas - 1)
                for m in range(1, GROUP):
                    split_high(pas, 0, m)
                groups(act, 1, GROUPS, lambda g, m: split_high(pas, g, m))
            evacuate(2)

        @block.tensor
        def _(pe):
            def product(k, stationary, part, start=False, stop=False):
                cols = slice((k % HALF_BANKS) * BANK, (k % HALF_BANKS + 1) * BANK)
                return pe.matmul(psum[k][:, :], stationary[:, :], part[:, cols], start=start, stop=stop)

            def products(pas, g, m, first=False):
                pe.wait_ge(stat_ready, g * GROUP + (pas * TILES + m + 1))
                for h in range(HALVES):
                    u = (g * GROUP + (pas * TILES + m)) * HALVES + h
                    slot = (m * HALVES + h) % SPLIT
                    banks = range(h * HALF_BANKS, (h + 1) * HALF_BANKS)
                    if first and pas:
                        pe.wait_ge(bank_read, (pas - 1) * BANKS + (h + 1) * HALF_BANKS)
                    pe.wait_ge(high_ready, u + 1)
                    for k in banks:
                        product(k, stat_low[m], high[slot], start=first)
                    for k in banks:
                        product(k, stat_high[m], high[slot])
                    pe.wait_ge(low_ready, u + 1)
                    for k in banks:
                        mm = product(k, stat_high[m], low[slot])
                    mm.then_inc(products_done, 1)

            def turn(pas, n):
                k, c = turn_order(pas)[n], pas * BANKS + n
                pe.wait_ge(evacuated, c + 1)
                for m in range(GROUP):
                    cols = slice(m * P, (m + 1) * P)
                    if pas < 2:
                        mm = pe.transpose(psum[k][:, cols], evac[c % EVAC][:, cols], identity[:, :])
                    else:
                        mm = pe.matmul(psum[k][:, cols], evac[c % EVAC][:, cols], w_t_sb[:, :],
                                       start=True, stop=True)
                mm.then_inc(turned, 1)

            def last_products(pas):
                m = GROUP - 1
                pe.wait_ge(stat_ready, (pas + 1) * TILES)
                for n, k in enumerate(turn_order(pas)):
                    h = n // HALF_BANKS
                    slot = (m * HALVES + h) % SPLIT
                    u = (pas + 1) * LAST - HALVES + h
                    if n % HALF_BANKS == 0:
                        pe.wait_ge(high_ready, u + 1)
                    product(k, stat_low[m], high[slot])
                    product(k, stat_high[m], high[slot])
                    if n % HALF_BANKS == 0:
                        pe.wait_ge(low_ready, u + 1)
                    mm = product(k, stat_high[m], low[slot], stop=True)
                    mm.then_inc(products_done if n % HALF_BANKS == HALF_BANKS - 1 else bank_done, 1)
                    if n >= TURN_LAG:
                        turn(pas, n - TURN_LAG)
                for n in range(BANKS - TURN_LAG, BANKS):
                    turn(pas, n)

            pe.wait_ge(constants_ready, 3)
            for pas in range(3):
                if pas == 2:
                    pe.wait_ge(weights_loaded, 32)
                for m in range(GROUP):
                    products(pas, 0, m, first=(m == 0))
                groups(pe, 1, GROUPS - 1, lambda g, m: products(pas, g, m))
                for m in range(GROUP - 1):
                    products(pas, GROUPS - 1, m)
                last_products(pas)

        @block.gpsimd
        def _(pool):
            pool.memset(minus_half[:, :], -0.5).then_inc(constants_ready, 1)
            pool.memset(identity[:, :], 0.0).then_inc(constants_ready, 1)
            pool.wait_ge(constants_ready, 2)
            pool.affine_select(out=identity[:, :], in_=identity[:, :], compare_op=ALU.not_equal, fill=1.0,
                               base=0, pattern=[[-1, P]], channel_multiplier=1)\
                .then_inc(constants_ready, 1)

            def split_stationary(pas, g, m):
                source = nodes if pas == 0 else scaled
                tile = g * GROUP + (m + first_tile(pas))
                q = g * GROUP + (pas * TILES + m)
                if isinstance(tile, int):
                    tile %= TILES
                rows = source[:, bass.ds(tile, 1), :].rearrange("p a c -> p (a c)")
                pool.wait_ge(x_loaded, 16)
                if not (pas == 0 and isinstance(g, int) and g == 0):
                    pool.wait_ge(products_done, (q - (STAT - 1)) * HALVES)
                pool.tensor_copy(stat_high[m][:, :], rows)
                pool.drain()
                pool.tensor_tensor(stat_low[m][:, :], rows, stat_high[m][:, :].bitcast(fp32), ALU.subtract)\
                    .then_inc(stat_ready, 1)

            def rstds(c):
                pool.wait_ge(var_ready, c + 1)
                pool.tensor_tensor(rstd[:, c % 2, :], var_eps[:, c % 2, :], minus_half[:, 0:GROUP], ALU.pow)\
                    .then_inc(rstd_ready, 1)

            def scale_rows(k):
                tiles = slice(k * GROUP, (k + 1) * GROUP)
                pool.wait_ge(normed, k + 1)
                pool.tensor_tensor(scaled[:, tiles, :], nodes[:, tiles, :],
                                   d_inv[:, tiles].unsqueeze(2).broadcast_to([P, GROUP, C]), ALU.mult)\
                    .then_inc(scaled_ready, 1)
                pool.wait_ge(scaled_ready, k + 1)

            pool.wait_ge(x_loaded, 16)
            for m in range(GROUP):
                split_stationary(0, 0, m)
            pool.wait_ge(x_rest_loaded, 16)
            groups(pool, 1, GROUPS, lambda g, m: split_stationary(0, g, m))
            pool.wait_ge(bank_read, 1)
            for m in range(GROUP):
                split_stationary(1, 0, m)
            pool.wait_ge(row_step, 4)
            pool.tensor_tensor(row_pow[:, :], row_safe[:, :], minus_half[:, :], ALU.pow).then_inc(row_pow_ready, 1)
            pool.wait_ge(bank_read, BANKS)
            groups(pool, 1, GROUPS - 1, lambda g, m: split_stationary(1, g, m))
            for m in range(GROUP):
                split_stationary(1, GROUPS - 1, m)
            pool.wait_ge(d_inv_ready, 1)
            rstds(0)
            scale_rows(0)
            for m in range(GROUP):
                split_stationary(2, 0, m)
            for k in range(1, BANKS):
                rstds(k)
                scale_rows(k)
                tile = k + GROUP - 1
                split_stationary(2, tile // GROUP, tile % GROUP)
            for tile in range(BANKS + GROUP - 1, PEELED * GROUP):
                split_stationary(2, tile // GROUP, tile % GROUP)
            pool.wait_ge(weights_loaded, 32)
            for k in range(BANKS):
                rows = nodes[:, k * GROUP:(k + 1) * GROUP, :]
                pool.tensor_tensor(rows, rows, bias_row[:, :].unsqueeze(1).broadcast_to([P, GROUP, C]), ALU.add)\
                    .then_inc(bias_added, 1)
            groups(pool, PEELED, GROUPS, lambda g, m: split_stationary(2, g, m))
            for k in range(BANKS):
                rstds(BANKS + k)

        @block.vector
        def _(dve):
            dve.wait_ge(small_loaded, 32)
            dve.tensor_scalar(t_eff[:, :], t_sb[:, :], 1e-8, -1.0, ALU.max, ALU.mult).then_inc(decay_step, 1)
            dve.wait_ge(decay_step, 1)
            dve.tensor_scalar(decay[:, :], evals_sb[:, :], t_eff[:, 0:1], None, ALU.mult).then_inc(decay_step, 1)

            def split_low(pas, g, m, h):
                u = (g * GROUP + (pas * TILES + m)) * HALVES + h
                slot = (m * HALVES + h) % SPLIT
                dve.wait_ge(high_ready, u + 1)
                dve.tensor_tensor(low[slot][:, :], raw[m][:, h * HALF:(h + 1) * HALF],
                                  high[slot][:, :].bitcast(fp32), ALU.subtract).then_inc(low_ready, 1)

            def split_tile(pas, g, m):
                for h in range(HALVES):
                    split_low(pas, g, m, h)

            steps = [0]

            def step_done(instruction):
                instruction.then_inc(norm_step, 1)
                steps[0] += 1
                dve.wait_ge(norm_step, steps[0])

            def row_stats(c, rows):
                s = c % 2
                for m in range(GROUP):
                    last = dve.bn_stats(stats[:, s, m, :], rows[:, m, :])
                step_done(last)
                for m in range(GROUP):
                    last = dve.bn_aggr(moments[:, s, m, :], stats[:, s, m, :])
                step_done(last)
                dve.tensor_scalar(var_eps[:, s, :], moments[:, s, :, 1], EPS, None, ALU.add)\
                    .then_inc(var_ready, 1)

            def normalise(c, rows, to):
                s = c % 2
                dve.wait_ge(rstd_ready, c + 1)
                for m in range(GROUP):
                    last = dve.tensor_scalar(to[:, m, :], rows[:, m, :], moments[:, s, m, 0:1],
                                             rstd[:, s, m:m + 1], ALU.subtract, ALU.mult)
                return last

            def bank(k):
                return psum[k][:, :].rearrange("p (m c) -> p m c", m=GROUP)

            def bank_tiles(k):
                return slice(k * GROUP, (k + 1) * GROUP)

            groups(dve, 0, GROUPS, lambda g, m: split_tile(0, g, m))
            split_tile(1, 0, 0)

            dve.wait_ge(coefs_ready, 1)
            for n, k in enumerate(turn_order(0)):
                tiles = bank_tiles(k)
                dve.wait_ge(turned, n + 1)
                dve.tensor_tensor(scaled[:, tiles, :], bank(k),
                                  coefs[:, tiles].unsqueeze(2).broadcast_to([P, GROUP, C]), ALU.mult)\
                    .then_inc(bank_read, 1)

            for m in range(1, GROUP):
                split_tile(1, 0, m)
            dve.tensor_tensor(row_sum[:, :], row_parts[:, :, 0], row_parts[:, :, 1], ALU.add).then_inc(row_step, 1)
            dve.wait_ge(row_step, 1)
            dve.tensor_scalar(row_zero[:, :], row_sum[:, :], 0.0, None, ALU.is_equal).then_inc(row_step, 1)
            dve.tensor_scalar(row_keep[:, :], row_sum[:, :], 0.0, None, ALU.not_equal).then_inc(row_step, 1)
            dve.wait_ge(row_step, 3)
            dve.tensor_tensor(row_safe[:, :], row_sum[:, :], row_zero[:, :], ALU.add).then_inc(row_step, 1)
            groups(dve, 1, GROUPS, lambda g, m: split_tile(1, g, m))
            dve.wait_ge(row_pow_ready, 1)
            dve.tensor_tensor(d_inv[:, :], row_pow[:, :], row_keep[:, :], ALU.mult).then_inc(d_inv_ready, 1)
            split_tile(2, 0, 0)

            def add_bank(k):
                rows = nodes[:, bank_tiles(k), :]
                dve.wait_ge(turned, BANKS + k + 1)
                dve.tensor_tensor(rows, bank(k), rows, ALU.add).then_inc(bank_read, 1)

            add_bank(0)
            dve.wait_ge(bank_read, BANKS + 1)
            row_stats(0, nodes[:, bank_tiles(0), :])
            for k in range(1, BANKS):
                add_bank(k)
                if k == 2:
                    normalise(0, nodes[:, bank_tiles(0), :], nodes[:, bank_tiles(0), :]).then_inc(normed, 1)
            dve.wait_ge(bank_read, 2 * BANKS)
            for tile in range(1, PEELED * GROUP):
                split_low(2, tile // GROUP, tile % GROUP, 0)
                if tile < BANKS:
                    row_stats(tile, nodes[:, bank_tiles(tile), :])
                split_low(2, tile // GROUP, tile % GROUP, 1)
                if tile < BANKS:
                    rows = nodes[:, bank_tiles(tile), :]
                    normalise(tile, rows, rows).then_inc(normed, 1)
            groups(dve, PEELED, GROUPS, lambda g, m: split_tile(2, g, m))

            def last_sums(k):
                rows = scaled[:, bank_tiles(k), :]
                dve.wait_ge(turned, 2 * BANKS + k + 1)
                for m in range(GROUP):
                    tile = k * GROUP + m
                    last = dve.scalar_tensor_tensor(out=rows[:, m, :], in0=bank(k)[:, m, :],
                                                    scalar=d_inv[:, tile:tile + 1], in1=nodes[:, tile, :],
                                                    op0=ALU.mult, op1=ALU.add)
                step_done(last)
                row_stats(BANKS + k, rows)

            def last_rows(k):
                if k >= 2:
                    dve.wait_ge(stored[k % 2], 16 * (k // 2))
                normalise(BANKS + k, scaled[:, bank_tiles(k), :], result[k % 2][:, :, :])\
                    .then_inc(result_ready, 1)

            dve.wait_ge(bias_added, BANKS)
            for k in range(BANKS):
                last_sums(k)
                if k:
                    last_rows(k - 1)
            last_rows(BANKS - 1)


def kernel(**inputs):
    import numpy as _np
    import concourse.bacc as _bacc
    from concourse import mybir as _mybir
    from concourse.bass_utils import run_bass_kernel_spmd as _run

    x, adj = _np.asarray(inputs["x"]), _np.asarray(inputs["adj"])
    n, c = x.shape
    partitions = 128
    laid_out = {
        "x": x,
        "adj": adj,
        "adj_t": adj.T,
        "evals": _np.asarray(inputs["L0_gnn_evals"]).reshape(n // partitions, partitions).T,
        "t": _np.asarray(inputs["L0_gnn_t"]),
        "w_t": _np.asarray(inputs["L1_gnn_W"]).T,
        "b": _np.asarray(inputs["L1_gnn_b"]),
    }
    nc = _bacc.Bacc("TRN2", target_bir_lowering=False, num_devices=1)
    arrays, args = {}, []
    for name, a in laid_out.items():
        a = _np.ascontiguousarray(a)
        arrays[f"in_{name}_dram"] = a
        args.append(nc.dram_tensor(f"in_{name}_dram", a.shape, _mybir.dt.from_np(a.dtype), kind="ExternalInput").ap())
    args.append(nc.dram_tensor("out_0_dram", (n, c), _mybir.dt.float32, kind="ExternalOutput").ap())
    spectral_gcn_kernel(nc, *args)
    r = _run(nc, [arrays], core_ids=[0])
    return r.results[0]["out_0_dram"]
```

```python
import concourse.bass as bass
from concourse import mybir
from contextlib import ExitStack


def spectral_gcn_kernel(
    nc: bass.Bass,
    x: bass.AP,
    adj: bass.AP,
    adj_t: bass.AP,
    evals: bass.AP,
    t: bass.AP,
    w_t: bass.AP,
    b: bass.AP,
    out: bass.AP,
):
    fp32 = mybir.dt.float32
    fp32r = mybir.dt.float32r
    ALU = mybir.AluOpType
    ACT = mybir.ActivationFunctionType

    P = nc.NUM_PARTITIONS
    N, C = x.shape
    TILES = N // P
    BANKS = 8
    BANK = N // BANKS
    GROUP = BANK // P
    GROUPS = TILES // GROUP
    RAW = 8
    ROUNDS = TILES // RAW
    HALVES = 2
    HALF = N // HALVES
    HALF_BANKS = BANKS // HALVES
    UNITS = TILES * HALVES
    HIGHS = 4
    LOWS = 2
    STAT = GROUP
    X_AT = 3
    EVAC = 2
    NORMS = 4
    EARLY = 2 * RAW
    TURN_LAG = 2
    STAT_AT = (3, 4)
    SPLITS_AT = ((3, 7), (4, 7))
    EPS = 1e-5

    x_v = x.rearrange("(t p) c -> p t c", p=P)
    out_v = out.rearrange("(t p) c -> p t c", p=P)

    ctx = ExitStack()
    with ctx:
        def sb(name, shape, dt=fp32):
            return ctx.enter_context(nc.sbuf_tensor(name, shape, dt))

        def sem(name):
            return ctx.enter_context(nc.semaphore(name))

        raw = [sb(f"raw{s}", [P, N]) for s in range(RAW)]
        high = [sb(f"high{s}", [P, HALF], fp32r) for s in range(HIGHS)]
        low = [sb(f"low{s}", [P, HALF], fp32r) for s in range(LOWS)]
        stat_high = [sb(f"stat_high{s}", [P, C], fp32r) for s in range(STAT)]
        stat_low = [sb(f"stat_low{s}", [P, C], fp32r) for s in range(STAT)]
        nodes = sb("nodes", [P, TILES, C])
        evac = [sb(f"evac{s}", [P, BANK]) for s in range(EVAC)]
        identity = sb("identity", [P, P])
        w_t_sb = sb("w_t_sb", [C, C])
        bias_row = sb("bias_row", [P, C])
        evals_sb = sb("evals_sb", [P, TILES])
        t_sb = sb("t_sb", [P, 1])
        t_eff = sb("t_eff", [P, 1])
        decay = sb("decay", [P, TILES])
        coefs = sb("coefs", [P, TILES])
        row_parts = sb("row_parts", [P, TILES, HALVES])
        row_sum = sb("row_sum", [P, TILES])
        row_zero = sb("row_zero", [P, TILES])
        row_safe = sb("row_safe", [P, TILES])
        row_keep = sb("row_keep", [P, TILES])
        row_pow = sb("row_pow", [P, TILES])
        d_inv = sb("d_inv", [P, TILES])
        minus_half = sb("minus_half", [P, TILES])
        stats = sb("stats", [P, NORMS, GROUP, 6])
        moments = sb("moments", [P, NORMS, GROUP, 2])
        minus_mean = sb("minus_mean", [P, NORMS, GROUP])
        var_eps = sb("var_eps", [P, NORMS, GROUP])
        rstd = sb("rstd", [P, NORMS, GROUP])
        shift = sb("shift", [P, NORMS, GROUP])

        psum = [ctx.enter_context(nc.psum_tensor(f"bank{k}", [P, BANK], fp32)) for k in range(BANKS)]

        x_loaded = sem("x_loaded")
        x_rest_loaded = sem("x_rest_loaded")
        x_back = [sem(f"x_back{s}") for s in range(2)]
        small_loaded = sem("small_loaded")
        weights_loaded = sem("weights_loaded")
        raw_loaded = [[sem(f"raw_loaded{s}_{h}") for h in range(HALVES)] for s in range(RAW)]
        high_ready = sem("high_ready")
        low_ready = sem("low_ready")
        stat_high_ready = sem("stat_high_ready")
        stat_ready = sem("stat_ready")
        products_done = sem("products_done")
        constants_ready = sem("constants_ready")
        decay_step = sem("decay_step")
        coefs_ready = sem("coefs_ready")
        bank_done = sem("bank_done")
        evacuated = sem("evacuated")
        turned = sem("turned")
        bank_read = sem("bank_read")
        row_step = sem("row_step")
        row_pow_ready = sem("row_pow_ready")
        d_inv_ready = sem("d_inv_ready")
        norm_step = sem("norm_step")
        var_ready = sem("var_ready")
        rstd_ready = sem("rstd_ready")
        tile_normed = sem("tile_normed")
        normed = sem("normed")
        bias_added = sem("bias_added")
        result_ready = sem("result_ready")
        last_half_ready = sem("last_half_ready")
        stored = sem("stored")

        block = ctx.enter_context(nc.Block())

        def first_tile(pas):
            return RAW if pas == 1 else 0

        def turn_order(pas):
            first = first_tile(pas + 1) // GROUP
            return [first] + [k for k in range(BANKS) if k != first]

        def tiles_of(k):
            return slice(k * GROUP, (k + 1) * GROUP)

        def stationary_rows(pas, j):
            tile = j + first_tile(pas)
            if isinstance(tile, int):
                tile %= TILES
            return nodes[:, bass.ds(tile, 1), :].rearrange("p a c -> p (a c)"), tile

        def loop(engine, start, end, tiles, body):
            with engine.Fori(start, end) as i:
                for m in range(tiles):
                    body(i, m, i * tiles + m)

        def peeled(start, end, tiles, body):
            for j in range(start, end):
                body(j // tiles, j % tiles, j)

        @block.sync
        def _(sp):
            def load(source, pas, m, j, row):
                for h in range(HALVES):
                    if not (pas == 0 and isinstance(j, int)):
                        sp.wait_ge(low_ready, (j + (pas * TILES - RAW)) * HALVES + h + 1)
                    cols = slice(h * HALF, (h + 1) * HALF)
                    sp.dma_start(raw[m][:, cols], source[bass.ds(row, P), cols]).then_inc(raw_loaded[m][h], 16)

            sp.dma_start(nodes[:, tiles_of(0), :], x_v[:, tiles_of(0), :]).then_inc(x_loaded, 16)
            peeled(0, X_AT, RAW, lambda i, m, j: load(adj, 0, m, j, j * P))
            sp.dma_start(nodes[:, GROUP:TILES, :], x_v[:, GROUP:TILES, :]).then_inc(x_rest_loaded, 16)
            peeled(X_AT, RAW, RAW, lambda i, m, j: load(adj, 0, m, j, j * P))
            loop(sp, 1, ROUNDS, RAW, lambda i, m, j: load(adj, 0, m, j, j * P))
            loop(sp, 0, ROUNDS - 1, RAW, lambda i, m, j: load(adj_t, 1, m, j, (j + RAW) * P))
            for m in range(RAW):
                load(adj_t, 1, m, TILES - RAW + m, m * P)
            sp.wait_ge(stat_ready, 2 * TILES)
            retained = slice(0, RAW)
            sp.dma_start(nodes[:, retained, :], x_v[:, retained, :]).then_inc(x_back[0], 16)
            sp.dma_start(nodes[:, RAW:TILES, :], x_v[:, RAW:TILES, :]).then_inc(x_back[1], 16)
            loop(sp, 1, ROUNDS, RAW, lambda i, m, j: load(adj_t, 2, m, j, j * P))
            for k in range(BANKS):
                sp.wait_ge(result_ready, k + 1)
                if k == BANKS - 1:
                    sp.wait_ge(last_half_ready, 1)
                sp.dma_start(out_v[:, tiles_of(k), :], nodes[:, tiles_of(k), :]).then_inc(stored, 16)
            sp.wait_ge(stored, 16 * BANKS)

        @block.scalar
        def _(act):
            act.dma_start(evals_sb[:, :], evals).then_inc(small_loaded, 16)
            act.dma_start(t_sb[:, :], t.partition_broadcast(P)).then_inc(small_loaded, 16)
            act.dma_start(w_t_sb[:, :], w_t).then_inc(weights_loaded, 16)
            act.dma_start(bias_row[:, :], b.partition_broadcast(P)).then_inc(weights_loaded, 16)
            act.wait_ge(decay_step, 2)
            act.activation(coefs[:, :], decay[:, :], ACT.Exp).then_inc(coefs_ready, 1)

            def split_high(pas, i, m, j, halves=range(HALVES)):
                very_first = pas == 0 and isinstance(j, int)
                filled = (1, 1 + ROUNDS, 2 * ROUNDS)[pas] + i
                for h in halves:
                    act.wait_ge(raw_loaded[m][h], 16 * filled)
                    slot = (m * HALVES + h) % HIGHS
                    u = (j + pas * TILES) * HALVES + h
                    if not (very_first and u < HIGHS):
                        act.wait_ge(products_done, u - (HIGHS - 1))
                    piece = raw[m][:, h * HALF:(h + 1) * HALF]
                    if pas == 0:
                        act.activation(high[slot][:, :], piece, ACT.Copy,
                                       accum_out=row_parts[:, bass.ds(j, 1), h]).then_inc(high_ready, 1)
                    else:
                        act.activation(high[slot][:, :], piece, ACT.Copy).then_inc(high_ready, 1)

            def stat_high_part(pas, m, j):
                rows, tile = stationary_rows(pas, j)
                act.wait_ge(x_loaded, 16)
                if not (pas == 0 and isinstance(j, int) and j < STAT):
                    act.wait_ge(products_done, (j + (pas * TILES - STAT + 1)) * HALVES)
                scale = d_inv[:, bass.ds(tile, 1)] if pas == 2 else 1.0
                act.activation(stat_high[m % STAT][:, :], rows, ACT.Copy, scale=scale)\
                    .then_inc(stat_high_ready, 1)

            def split_tile(pas, i, m, j):
                stat_high_part(pas, m, j)
                split_high(pas, i, m, j)

            def evacuate(pas):
                for n, k in enumerate(turn_order(pas)):
                    c = pas * BANKS + n
                    h, behind = divmod(n, HALF_BANKS)
                    if behind == HALF_BANKS - 1:
                        act.wait_ge(products_done, (pas + 1) * UNITS - HALVES + h + 1)
                    else:
                        act.wait_ge(bank_done, (pas * HALVES + h) * (HALF_BANKS - 1) + behind + 1)
                    if c >= EVAC:
                        act.wait_ge(turned, c - EVAC + 1)
                    act.activation(evac[c % EVAC][:, :], psum[k][:, :], ACT.Copy).then_inc(evacuated, 1)
                    if pas < 2 and n == STAT_AT[pas]:
                        act.wait_ge((bank_read, tile_normed)[pas], 1)
                        stat_high_part(pas + 1, 0, 0)
                    if pas == 1 and n == HALF_BANKS - 1:
                        split_high(2, 0, 0, 0, halves=[0])

            def normalise(c, k, start=0, end=GROUP):
                act.wait_ge(rstd_ready, c + 1)
                for m in range(start, end):
                    rows = nodes[:, k * GROUP + m, :]
                    last = act.activation(rows, rows, ACT.Identity, bias=shift[:, c % NORMS, m:m + 1],
                                          scale=rstd[:, c % NORMS, m:m + 1])
                return last

            act.wait_ge(x_loaded, 16)
            peeled(0, GROUP, RAW, lambda i, m, j: split_tile(0, i, m, j))
            act.wait_ge(x_rest_loaded, 16)
            peeled(GROUP, RAW, RAW, lambda i, m, j: split_tile(0, i, m, j))
            loop(act, 1, ROUNDS, RAW, lambda i, m, j: split_tile(0, i, m, j))
            split_high(1, 0, 0, 0, halves=[0])
            evacuate(0)
            split_high(1, 0, 0, 0, halves=[1])
            act.wait_ge(bank_read, BANKS)
            peeled(1, RAW, RAW, lambda i, m, j: split_tile(1, i, m, j))
            loop(act, 1, ROUNDS - 1, RAW, lambda i, m, j: split_tile(1, i, m, j))
            peeled(TILES - RAW, TILES, RAW, lambda i, m, j: split_tile(1, i, m, j))
            act.wait_ge(d_inv_ready, 1)
            evacuate(1)
            split_high(2, 0, 0, 0, halves=[1])
            normalise(0, 0, start=1).then_inc(normed, 1)
            for j in range(1, EARLY):
                act.wait_ge(normed, j // GROUP + 1)
                split_tile(2, j // RAW, j % RAW, j)
                k, rest = divmod(j, 2)
                if rest == 0 and k < BANKS:
                    normalise(k, k).then_inc(normed, 1)
            act.wait_ge(normed, BANKS)
            loop(act, EARLY // RAW, ROUNDS, RAW, lambda i, m, j: split_tile(2, i, m, j))
            evacuate(2)
            for k in range(BANKS - 1):
                normalise(BANKS + k, k).then_inc(result_ready, 1)
            normalise(2 * BANKS - 1, BANKS - 1, end=GROUP // 2).then_inc(result_ready, 1)

        @block.tensor
        def _(pe):
            def product(k, stationary, part, start=False, stop=False):
                cols = slice((k % HALF_BANKS) * BANK, (k % HALF_BANKS + 1) * BANK)
                return pe.matmul(psum[k][:, :], stationary[:, :], part[:, cols], start=start, stop=stop)

            def products(pas, m, j, first=False):
                pe.wait_ge(stat_ready, j + (pas * TILES + 1))
                for h in range(HALVES):
                    u = (j + pas * TILES) * HALVES + h
                    high_slot, low_slot = (m * HALVES + h) % HIGHS, (m * HALVES + h) % LOWS
                    banks = range(h * HALF_BANKS, (h + 1) * HALF_BANKS)
                    if first and pas:
                        pe.wait_ge(bank_read, (pas - 1) * BANKS + (h + 1) * HALF_BANKS)
                    pe.wait_ge(high_ready, u + 1)
                    for k in banks:
                        product(k, stat_low[m], high[high_slot], start=first)
                    for k in banks:
                        product(k, stat_high[m], high[high_slot])
                    pe.wait_ge(low_ready, u + 1)
                    for k in banks:
                        mm = product(k, stat_high[m], low[low_slot])
                    mm.then_inc(products_done, 1)

            def turn(pas, n):
                k, c = turn_order(pas)[n], pas * BANKS + n
                pe.wait_ge(evacuated, c + 1)
                for m in range(GROUP):
                    cols = slice(m * P, (m + 1) * P)
                    if pas < 2:
                        mm = pe.transpose(psum[k][:, cols], evac[c % EVAC][:, cols], identity[:, :])
                    else:
                        mm = pe.matmul(psum[k][:, cols], evac[c % EVAC][:, cols], w_t_sb[:, :],
                                       start=True, stop=True)
                mm.then_inc(turned, 1)

            def last_products(pas):
                m = GROUP - 1
                pe.wait_ge(stat_ready, (pas + 1) * TILES)
                for n, k in enumerate(turn_order(pas)):
                    h = n // HALF_BANKS
                    high_slot, low_slot = (m * HALVES + h) % HIGHS, (m * HALVES + h) % LOWS
                    u = (pas + 1) * UNITS - HALVES + h
                    if n % HALF_BANKS == 0:
                        pe.wait_ge(high_ready, u + 1)
                    product(k, stat_low[m], high[high_slot])
                    product(k, stat_high[m], high[high_slot])
                    if n % HALF_BANKS == 0:
                        pe.wait_ge(low_ready, u + 1)
                    mm = product(k, stat_high[m], low[low_slot], stop=True)
                    mm.then_inc(products_done if n % HALF_BANKS == HALF_BANKS - 1 else bank_done, 1)
                    if n >= TURN_LAG:
                        turn(pas, n - TURN_LAG)
                for n in range(BANKS - TURN_LAG, BANKS):
                    turn(pas, n)

            pe.wait_ge(constants_ready, 3)
            for pas in range(3):
                if pas == 2:
                    pe.wait_ge(weights_loaded, 32)
                peeled(0, GROUP, GROUP, lambda i, m, j: products(pas, m, j, first=(j == 0)))
                loop(pe, 1, GROUPS - 1, GROUP, lambda i, m, j: products(pas, m, j))
                peeled(TILES - GROUP, TILES - 1, GROUP, lambda i, m, j: products(pas, m, j))
                last_products(pas)

        @block.gpsimd
        def _(pool):
            pool.memset(minus_half[:, :], -0.5).then_inc(constants_ready, 1)
            pool.memset(identity[:, :], 0.0).then_inc(constants_ready, 1)
            pool.wait_ge(constants_ready, 2)
            pool.affine_select(out=identity[:, :], in_=identity[:, :], compare_op=ALU.not_equal, fill=1.0,
                               base=0, pattern=[[-1, P]], channel_multiplier=1)\
                .then_inc(constants_ready, 1)

            def rstds(c):
                n = c % NORMS
                pool.wait_ge(var_ready, c + 1)
                if c - NORMS >= BANKS:
                    pool.wait_ge(result_ready, c - NORMS - BANKS + 1)
                elif c >= NORMS:
                    pool.wait_ge(normed, c - NORMS + 1)
                pool.tensor_scalar(minus_mean[:, n, :], moments[:, n, :, 0], -1.0, None, ALU.mult)
                pool.tensor_scalar(var_eps[:, n, :], moments[:, n, :, 1], EPS, None, ALU.add)
                pool.drain()
                pool.tensor_tensor(rstd[:, n, :], var_eps[:, n, :], minus_half[:, 0:GROUP], ALU.pow)
                pool.drain()
                pool.tensor_tensor(shift[:, n, :], minus_mean[:, n, :], rstd[:, n, :], ALU.mult)\
                    .then_inc(rstd_ready, 1)

            pool.wait_ge(row_step, 4)
            pool.tensor_tensor(row_pow[:, :], row_safe[:, :], minus_half[:, :], ALU.pow).then_inc(row_pow_ready, 1)
            for c in range(2 * BANKS):
                rstds(c)

        @block.vector
        def _(dve):
            dve.wait_ge(small_loaded, 32)
            dve.tensor_scalar(t_eff[:, :], t_sb[:, :], 1e-8, -1.0, ALU.max, ALU.mult).then_inc(decay_step, 1)
            dve.wait_ge(decay_step, 1)
            dve.tensor_scalar(decay[:, :], evals_sb[:, :], t_eff[:, 0:1], None, ALU.mult).then_inc(decay_step, 1)

            def split_low(pas, m, j, h):
                u = (j + pas * TILES) * HALVES + h
                high_slot, low_slot = (m * HALVES + h) % HIGHS, (m * HALVES + h) % LOWS
                dve.wait_ge(high_ready, u + 1)
                if not (isinstance(j, int) and u < LOWS):
                    dve.wait_ge(products_done, u - (LOWS - 1))
                dve.tensor_tensor(low[low_slot][:, :], raw[m][:, h * HALF:(h + 1) * HALF],
                                  high[high_slot][:, :].bitcast(fp32), ALU.subtract).then_inc(low_ready, 1)

            def stat_low_part(pas, m, j):
                rows, tile = stationary_rows(pas, j)
                high_part = stat_high[m % STAT][:, :].bitcast(fp32)
                dve.wait_ge(stat_high_ready, j + (pas * TILES + 1))
                if pas == 2:
                    low_part = dve.scalar_tensor_tensor(out=stat_low[m % STAT][:, :], in0=rows,
                                                        scalar=d_inv[:, bass.ds(tile, 1)], in1=high_part,
                                                        op0=ALU.mult, op1=ALU.subtract)
                else:
                    low_part = dve.tensor_tensor(stat_low[m % STAT][:, :], rows, high_part, ALU.subtract)
                low_part.then_inc(stat_ready, 1)

            def split_tile(pas, m, j):
                stat_low_part(pas, m, j)
                for h in range(HALVES):
                    split_low(pas, m, j, h)

            steps = [0]

            def step_done(instruction):
                instruction.then_inc(norm_step, 1)
                steps[0] += 1
                dve.wait_ge(norm_step, steps[0])

            def row_stats(c, rows):
                s = c % NORMS
                if c >= NORMS:
                    dve.wait_ge(rstd_ready, c - NORMS + 1)
                for m in range(GROUP):
                    last = dve.bn_stats(stats[:, s, m, :], rows[:, m, :])
                step_done(last)
                for m in range(GROUP):
                    last = dve.bn_aggr(moments[:, s, m, :], stats[:, s, m, :])
                last.then_inc(var_ready, 1)

            def bank(k):
                return psum[k][:, :].rearrange("p (m c) -> p m c", m=GROUP)

            def node_rows(k):
                return nodes[:, tiles_of(k), :]

            peeled(0, RAW, RAW, lambda i, m, j: split_tile(0, m, j))
            loop(dve, 1, ROUNDS, RAW, lambda i, m, j: split_tile(0, m, j))

            dve.wait_ge(coefs_ready, 1)
            dve.wait_ge(stat_ready, TILES)
            for n, k in enumerate(turn_order(0)):
                dve.wait_ge(turned, n + 1)
                dve.tensor_tensor(node_rows(k), bank(k),
                                  coefs[:, tiles_of(k)].unsqueeze(2).broadcast_to([P, GROUP, C]), ALU.mult)\
                    .then_inc(bank_read, 1)
                if n == STAT_AT[0]:
                    stat_low_part(1, 0, 0)
                if n in SPLITS_AT[0]:
                    split_low(1, 0, 0, SPLITS_AT[0].index(n))
            peeled(1, RAW, RAW, lambda i, m, j: split_tile(1, m, j))
            dve.tensor_tensor(row_sum[:, :], row_parts[:, :, 0], row_parts[:, :, 1], ALU.add).then_inc(row_step, 1)
            dve.wait_ge(row_step, 1)
            dve.tensor_scalar(row_zero[:, :], row_sum[:, :], 0.0, None, ALU.is_equal).then_inc(row_step, 1)
            dve.tensor_scalar(row_keep[:, :], row_sum[:, :], 0.0, None, ALU.not_equal).then_inc(row_step, 1)
            dve.wait_ge(row_step, 3)
            dve.tensor_tensor(row_safe[:, :], row_sum[:, :], row_zero[:, :], ALU.add).then_inc(row_step, 1)
            loop(dve, 1, ROUNDS - 1, RAW, lambda i, m, j: split_tile(1, m, j))
            dve.wait_ge(row_pow_ready, 1)
            dve.tensor_tensor(d_inv[:, :], row_pow[:, :], row_keep[:, :], ALU.mult).then_inc(d_inv_ready, 1)
            peeled(TILES - RAW, TILES, RAW, lambda i, m, j: split_tile(1, m, j))

            dve.wait_ge(x_back[0], 16)
            for n, k in enumerate(turn_order(1)):
                if n == RAW // GROUP:
                    dve.wait_ge(x_back[1], 16)
                dve.wait_ge(turned, BANKS + n + 1)
                dve.tensor_tensor(node_rows(k), bank(k), node_rows(k), ALU.add).then_inc(bank_read, 1)
                if n == 0:
                    dve.wait_ge(bank_read, BANKS + 1)
                    row_stats(0, node_rows(0))
                if n == 2:
                    dve.wait_ge(rstd_ready, 1)
                    dve.tensor_scalar(nodes[:, 0, :], nodes[:, 0, :], rstd[:, 0, 0:1], shift[:, 0, 0:1],
                                      ALU.mult, ALU.add).then_inc(tile_normed, 1)
                if n == STAT_AT[1]:
                    stat_low_part(2, 0, 0)
                if n in SPLITS_AT[1]:
                    split_low(2, 0, 0, SPLITS_AT[1].index(n))
            dve.wait_ge(bank_read, 2 * BANKS)
            for j in range(1, EARLY):
                stat_low_part(2, j % RAW, j)
                split_low(2, j % RAW, j, 0)
                k, rest = divmod(j + 1, 2)
                if rest == 0 and k < BANKS:
                    row_stats(k, node_rows(k))
                split_low(2, j % RAW, j, 1)
            dve.wait_ge(weights_loaded, 32)
            with dve.Fori(EARLY // RAW, ROUNDS) as i:
                for m in range(RAW):
                    split_tile(2, m, i * RAW + m)
                    if m % 2:
                        group = (i - EARLY // RAW) * GROUP + m // 2
                        rows = nodes[:, bass.ds(group * GROUP, GROUP), :]
                        dve.wait_ge(stat_ready, i * RAW + (2 * TILES + m + 1))
                        dve.tensor_tensor(rows, rows, bias_row[:, :].unsqueeze(1).broadcast_to([P, GROUP, C]),
                                          ALU.add).then_inc(bias_added, 1)

            dve.wait_ge(bias_added, BANKS)
            for k in range(BANKS):
                dve.wait_ge(turned, 2 * BANKS + k + 1)
                for m in range(GROUP):
                    tile = k * GROUP + m
                    last = dve.scalar_tensor_tensor(out=nodes[:, tile, :], in0=bank(k)[:, m, :],
                                                    scalar=d_inv[:, tile:tile + 1], in1=nodes[:, tile, :],
                                                    op0=ALU.mult, op1=ALU.add)
                step_done(last)
                row_stats(BANKS + k, node_rows(k))
            dve.wait_ge(rstd_ready, 2 * BANKS)
            s = (2 * BANKS - 1) % NORMS
            for m in range(GROUP // 2, GROUP):
                rows = nodes[:, (BANKS - 1) * GROUP + m, :]
                last = dve.tensor_scalar(rows, rows, rstd[:, s, m:m + 1], shift[:, s, m:m + 1],
                                         ALU.mult, ALU.add)
            last.then_inc(last_half_ready, 1)


def kernel(**inputs):
    import numpy as _np
    import concourse.bacc as _bacc
    from concourse import mybir as _mybir
    from concourse.bass_utils import run_bass_kernel_spmd as _run

    x, adj = _np.asarray(inputs["x"]), _np.asarray(inputs["adj"])
    n, c = x.shape
    partitions = 128
    laid_out = {
        "x": x,
        "adj": adj,
        "adj_t": adj.T,
        "evals": _np.asarray(inputs["L0_gnn_evals"]).reshape(n // partitions, partitions).T,
        "t": _np.asarray(inputs["L0_gnn_t"]),
        "w_t": _np.asarray(inputs["L1_gnn_W"]).T,
        "b": _np.asarray(inputs["L1_gnn_b"]),
    }
    nc = _bacc.Bacc("TRN2", target_bir_lowering=False, num_devices=1)
    arrays, args = {}, []
    for name, a in laid_out.items():
        a = _np.ascontiguousarray(a)
        arrays[f"in_{name}_dram"] = a
        args.append(nc.dram_tensor(f"in_{name}_dram", a.shape, _mybir.dt.from_np(a.dtype), kind="ExternalInput").ap())
    args.append(nc.dram_tensor("out_0_dram", (n, c), _mybir.dt.float32, kind="ExternalOutput").ap())
    spectral_gcn_kernel(nc, *args)
    r = _run(nc, [arrays], core_ids=[0])
    return r.results[0]["out_0_dram"]
```
